# Optimizing a Trainium2 kernel written in Bass

```python
import numpy as np
import jax
import jax.numpy as jnp

def _softmax(x, axis=-1):
    return jax.nn.softmax(x, axis=axis)

def _gelu(x):
    return jax.nn.gelu(x, approximate=True)

def _silu(x):
    return jax.nn.silu(x)

def _sigmoid(x):
    return jax.nn.sigmoid(x)

def _layernorm(x, axis=-1, eps=1e-05):
    m = jnp.mean(x, axis=axis, keepdims=True)
    v = jnp.var(x, axis=axis, keepdims=True)
    return (x - m) / jnp.sqrt(v + eps)

def _scatter_add(tgt, idx, src, axis=0):
    return tgt.at[idx].add(src)

def _segment_sum(src, seg, n):
    return jax.ops.segment_sum(src, seg, n)
kernel_name = 'mk_xattn_ffn_d1_seqx_r4_6b7252'

def setup_inputs(seed: int=0):
    np.random.seed(seed)
    _w = jnp.asarray

    def _rec_inputs():
        import jax
        import jax.numpy as jnp
        _rk = jax.random.key(seed)
        x = -0.000125 + 0.9999 * jax.random.normal(jax.random.fold_in(_rk, 1), (2, 512, 1024), jnp.float32)
        _lenS = 512 - jax.random.randint(jax.random.fold_in(_rk, 7), (2,), 0, max(1, 512 // 4) + 1, jnp.int32)
        _lenS2 = 1024 - jax.random.randint(jax.random.fold_in(_rk, 8), (2,), 0, max(1, 1024 // 4) + 1, jnp.int32)
        _ctx_4096P = jax.random.normal(jax.random.fold_in(_rk, 11), (2, 16, 1024), jnp.float32)
        _ctx_4096c = jax.random.dirichlet(jax.random.fold_in(_rk, 511), 0.3 * jnp.ones((16,), jnp.float32), (2, 1024))
        _ctx_4096t = jnp.einsum('bsk,bkd->bsd', _ctx_4096c, _ctx_4096P)
        _ctx_4096t = _ctx_4096t * jax.lax.rsqrt(jnp.mean(jnp.square(_ctx_4096t)) + 1e-12) * 0.953939
        ctx_4096 = -5.72187e-05 + 0.999849 * (_ctx_4096t + 0.3 * jax.random.normal(jax.random.fold_in(_rk, 611), (2, 1024, 1024), jnp.float32))
        return (x, ctx_4096)
    x, ctx_4096 = _rec_inputs()

    def _L0_xattn_setup():
        import jax, jax.numpy as jnp
        import numpy as np
        QMIN = 0.0
        QMAX = 255.0

        def fake_quant(x, scale, zp):
            s = scale.reshape(())
            z = zp.reshape(())
            q = jnp.clip(jnp.round(x / s + z), QMIN, QMAX)
            return (q - z) * s
        key = jax.random.key(seed)
        k1, k2 = jax.random.split(key)
        B, M, K, N = (4, 512, 1024, 1024)
        x1 = jax.random.normal(k1, (B, M, K), dtype=jnp.float32)
        x2 = jax.random.normal(k2, (B, K, N), dtype=jnp.float32)
        x1_scale = jnp.full((1,), 8.0 / 255.0, dtype=jnp.float32)
        x1_zp = jnp.full((1,), 128.0, dtype=jnp.float32)
        x2_scale = jnp.full((1,), 8.0 / 255.0, dtype=jnp.float32)
        x2_zp = jnp.full((1,), 128.0, dtype=jnp.float32)
        return {'x1': x1, 'x2': x2, 'x1_scale': x1_scale, 'x1_zp': x1_zp, 'x2_scale': x2_scale, 'x2_zp': x2_zp}
    _L0_xattn_all = _L0_xattn_setup()
    _L0_xattn_in = {k: v for k, v in _L0_xattn_all.items() if k in ('x1_scale', 'x1_zp', 'x2_scale', 'x2_zp')}
    del _L0_xattn_all

    def _L0_ffn_setup():
        import jax, jax.numpy as jnp
        import numpy as np
        B, S, D_IN, D_OUT = (2, 512, 1024, 1024)
        E, K, R = (8, 2, 16)
        SCALING = 32.0 / 16.0
        key = jax.random.key(seed)
        ks = jax.random.split(key, 6)
        x = jax.random.normal(ks[0], (B, S, D_IN), dtype=jnp.float32)
        gate_w = jax.random.normal(ks[1], (E, D_IN), dtype=jnp.float32) * 0.02
        base_w = jax.random.normal(ks[2], (D_OUT, D_IN), dtype=jnp.float32) * 0.02
        base_b = jax.random.normal(ks[3], (D_OUT,), dtype=jnp.float32) * 0.02
        lora_A = jax.random.normal(ks[4], (E, R, D_IN), dtype=jnp.float32) * 0.02
        lora_B = jax.random.normal(ks[5], (E, D_OUT, R), dtype=jnp.float32) * 0.02
        return {'x': x, 'gate_w': gate_w, 'base_w': base_w, 'base_b': base_b, 'lora_A': lora_A, 'lora_B': lora_B}
    _L0_ffn_all = _L0_ffn_setup()
    _L0_ffn_in = {k: v for k, v in _L0_ffn_all.items() if k in ('gate_w', 'base_w', 'base_b', 'lora_A', 'lora_B')}
    del _L0_ffn_all
    return {'x': x, 'ctx_4096': ctx_4096, 'L0_xattn_x1_scale': _L0_xattn_in['x1_scale'], 'L0_xattn_x1_zp': _L0_xattn_in['x1_zp'], 'L0_xattn_x2_scale': _L0_xattn_in['x2_scale'], 'L0_xattn_x2_zp': _L0_xattn_in['x2_zp'], 'L0_ffn_gate_w': _L0_ffn_in['gate_w'], 'L0_ffn_base_w': _L0_ffn_in['base_w'], 'L0_ffn_base_b': _L0_ffn_in['base_b'], 'L0_ffn_lora_A': _L0_ffn_in['lora_A'], 'L0_ffn_lora_B': _L0_ffn_in['lora_B']}

def reference(x, ctx_4096, L0_xattn_x1_scale, L0_xattn_x1_zp, L0_xattn_x2_scale, L0_xattn_x2_zp, L0_ffn_gate_w, L0_ffn_base_w, L0_ffn_base_b, L0_ffn_lora_A, L0_ffn_lora_B):
    import jax
    import jax.numpy as jnp

    def _L0_xattn_ref(x1, x2, x1_scale, x1_zp, x2_scale, x2_zp):
        import jax, jax.numpy as jnp
        import numpy as np
        QMIN = 0.0
        QMAX = 255.0

        def fake_quant(x, scale, zp):
            s = scale.reshape(())
            z = zp.reshape(())
            q = jnp.clip(jnp.round(x / s + z), QMIN, QMAX)
            return (q - z) * s
        q1 = fake_quant(x1, x1_scale, x1_zp)
        q2 = fake_quant(x2, x2_scale, x2_zp)
        return jnp.matmul(q1, q2)

    def _L0_ffn_ref(x, gate_w, base_w, base_b, lora_A, lora_B):
        import jax, jax.numpy as jnp
        import numpy as np
        B, S, D_IN, D_OUT = (2, 512, 1024, 1024)
        E, K, R = (8, 2, 16)
        SCALING = 32.0 / 16.0
        gate_logits = jnp.einsum('bsd,ed->bse', x, gate_w)
        weights, selected = jax.lax.top_k(gate_logits, K)
        weights = jax.nn.softmax(weights.astype(jnp.float32), axis=2).astype(x.dtype)
        result = jnp.einsum('bsd,od->bso', x, base_w) + base_b
        w_full = jnp.sum(jax.nn.one_hot(selected, E, dtype=x.dtype) * weights[..., None], axis=2)
        low = jnp.einsum('bsd,erd->ebsr', x, lora_A)
        lora_out = jnp.einsum('ebsr,eor,bse->bso', low, lora_B, w_full)
        result = result + SCALING * lora_out
        return result
    x = x + _L0_xattn_ref(_layernorm(x, axis=-1), ctx_4096, L0_xattn_x1_scale, L0_xattn_x1_zp, L0_xattn_x2_scale, L0_xattn_x2_zp)
    x = x + _L0_ffn_ref(_layernorm(x, axis=-1), L0_ffn_gate_w, L0_ffn_base_w, L0_ffn_base_b, L0_ffn_lora_A, L0_ffn_lora_B)
    return x

_drawn_inputs = setup_inputs


def setup_inputs(seed=0):
    import zlib

    import numpy as np

    out = dict(_drawn_inputs(seed))
    spreads = {}
    factors = {'L0_ffn_gate_w': 8.0, 'L0_ffn_base_b': 64.0, 'L0_ffn_lora_A': 8.0, 'L0_ffn_lora_B': 8.0}
    for name, (base, spread) in spreads.items():
        noise = np.random.default_rng([zlib.crc32(name.encode()), seed]).standard_normal(out[name].shape)
        drawn = base * np.exp(spread * noise) if base else spread * noise
        out[name] = jnp.asarray(drawn.astype(out[name].dtype))
    for name, factor in factors.items():
        out[name] = (out[name] * factor).astype(out[name].dtype)
    return out
```

```python
from contextlib import ExitStack

import concourse.bass as bass
from concourse import mybir

F32 = mybir.dt.float32
F32R = mybir.dt.float32r
BF16 = mybir.dt.bfloat16
U32 = mybir.dt.uint32
ALU = mybir.AluOpType
ACT = mybir.ActivationFunctionType

P = 128
HALF = 512
QMAX = 255.0
CENTRE = 128.0
ROUND = 1.5 * 2.0 ** 23
EPS = 1e-5
SCALING = 2.0
RING = 5


def xattn_ffn(nc, x, ctx, scales, w_t, ag_t, b_t, base_b, out):
    NB, S, D = x.shape
    S2 = ctx.shape[1]
    TILES = NB * S // P
    TPB = S // P
    KT = D // P
    CT = S2 // P
    AG = ag_t.shape[1] // KT
    ER = b_t.shape[0]
    E = AG - ER
    R = ER // E
    assert ER == P and D == 2 * HALF and CT == KT

    x_d = x.rearrange("b (t p) d -> (b t) p d", p=P)
    out_d = out.rearrange("b (t p) d -> (b t) p d", p=P)
    ctx_d = ctx.rearrange("b (k p) d -> (b k) p d", p=P)
    w_d = w_t.rearrange("(k p) o -> k p o", p=P)

    with ExitStack() as stack:
        def sb(name, shape, dt):
            return stack.enter_context(nc.sbuf_tensor(name, shape, dt))

        def psum(name, shape, dt=F32):
            return stack.enter_context(nc.psum_tensor(name, shape, dt))

        def sem(name):
            return stack.enter_context(nc.semaphore(name))

        x_sb = sb("x_sb", [P, TILES, D], F32)
        ring = sb("ring", [P, RING, KT * AG], F32)
        c2 = sb("c2", [P, CT, D], BF16)
        w_hi = sb("w_hi", [P, KT, D], F32R)
        w_lo = sb("w_lo", [P, KT, D], F32R)
        ag_hi = sb("ag_hi", [P, KT, AG], F32R)
        ag_lo = sb("ag_lo", [P, KT, AG], F32R)
        b_hi = sb("b_hi", [P, D], F32R)
        b_lo = sb("b_lo", [P, D], F32R)
        y = sb("y", [P, D], F32)
        yt_hi = sb("yt_hi", [P, 2, KT, P], F32R)
        yt_lo = sb("yt_lo", [P, 2, KT, P], F32R)
        xq = sb("xq", [P, 2, D], F32)
        c1 = sb("c1", [P, 2, D], BF16)
        c1t = sb("c1t", [P, 4, KT, P], BF16)
        zfix = sb("zfix", [P, D], F32)
        bias = sb("bias", [P, D], F32)
        csum = sb("csum", [P, D], F32R)
        ident_f = sb("ident_f", [P, P], F32)
        ident_b = sb("ident_b", [P, P], BF16)
        ones_b = sb("ones_b", [P, P], BF16)
        ones_r = sb("ones_r", [P, P], F32R)
        iota = sb("iota", [P, E], F32)
        low_w = sb("low_w", [P, ER], F32)
        lt_hi = sb("lt_hi", [P, P], F32R)
        lt_lo = sb("lt_lo", [P, P], F32R)
        q_in = sb("q_in", [P, 4], F32)
        q_rec = sb("q_rec", [P, 4], F32)
        q_d = sb("q_d", [P, 4], F32)
        q_ss = sb("q_ss", [P, 4], F32)
        stats = sb("stats", [P, 2, 6], F32)
        mv = sb("mv", [P, 2, TILES, 2], F32)
        ve = sb("ve", [P, 2, TILES], F32)
        ln_v = sb("ln_v", [P, 2, TILES], F32)
        r0 = sb("r0", [P, 2, TILES], F32)
        r_n = sb("r_n", [P, 2, TILES], F32)
        r_h = sb("r_h", [P, 2, TILES], F32)
        rstd = sb("rstd", [P, 2, TILES], F32)
        rowsum = sb("rowsum", [P, TILES], F32)
        rowfix = sb("rowfix", [P, TILES], F32)
        lg = sb("lg", [P, E], F32)
        top = sb("top", [P, 8], F32)
        top_i = sb("top_i", [P, 8], U32)
        top_f = sb("top_f", [P, 2], F32)
        ex = sb("ex", [P, 1], F32)
        den = sb("den", [P, 1], F32)
        wts = sb("wts", [P, 2], F32)
        hot = sb("hot", [P, 3, E], F32)

        ps_even = [psum(f"ps_even{h}", [P, HALF]) for h in range(2)]
        ps_odd = [psum(f"ps_odd{h}", [P, HALF]) for h in range(2)]
        ps_att = [psum(f"ps_att{h}", [P, HALF]) for h in range(2)]
        ps_t = psum("ps_t", [P, HALF])
        ps_g = psum("ps_g", [P, HALF])
        ffn_bank = [ps_even, ps_odd]

        def att_bank(t):
            return ps_odd if t < TPB and t % 2 else ps_att

        ps_tb = ps_t[:, :].bitcast(BF16)
        low_t = ps_g[:, 256:256 + P]

        x_in = [sem(f"x_in{t}") for t in range(TILES)]
        ring_in = [sem(f"ring_in{r}") for r in range(RING)]
        q_loaded = sem("q_loaded")
        bias_in = sem("bias_in")
        stored = sem("stored")
        consts = sem("consts")
        q_ready = sem("q_ready")
        dve_step = sem("dve_step")
        pool_step = sem("pool_step")
        var_ready = [sem(f"var_ready{i}") for i in range(2)]
        logv_ready = [sem(f"logv_ready{i}") for i in range(2)]
        r0_ready = [sem(f"r0_ready{i}") for i in range(2)]
        xn_ready = sem("xn_ready")
        xrelu_ready = sem("xrelu_ready")
        xround_ready = sem("xround_ready")
        c1_ready = sem("c1_ready")
        c1t_psum = sem("c1t_psum")
        c1t_ready = sem("c1t_ready")
        crelu_ready = sem("crelu_ready")
        cround_ready = sem("cround_ready")
        c2_ready = sem("c2_ready")
        csum_ready = sem("csum_ready")
        colsum_psum = sem("colsum_psum")
        zfix_ready = sem("zfix_ready")
        att_done = sem("att_done")
        att_taken = sem("att_taken")
        x1_ready = sem("x1_ready")
        y_ready = sem("y_ready")
        xb_ready = sem("xb_ready")
        yt_psum = sem("yt_psum")
        yhi_ready = sem("yhi_ready")
        ylo_ready = sem("ylo_ready")
        ag_hi_ready = sem("ag_hi_ready")
        ag_ready = sem("ag_ready")
        whi_ready = sem("whi_ready")
        wlo_ready = sem("wlo_ready")
        bhi_ready = sem("bhi_ready")
        blo_ready = sem("blo_ready")
        ag_done = sem("ag_done")
        top_ready = sem("top_ready")
        ex_ready = sem("ex_ready")
        loww_ready = sem("loww_ready")
        lowt_psum = sem("lowt_psum")
        lthi_ready = sem("lthi_ready")
        ltlo_ready = sem("ltlo_ready")
        ffn_done = sem("ffn_done")
        rowfix_ready = sem("rowfix_ready")
        out_ready = sem("out_ready")

        ss, ssd1, ssd2, ssdd = (q_ss[:, i:i + 1] for i in range(4))

        loads = [("c", k) for k in range(CT)] + [("a", 0)] + [("w", k) for k in range(KT)] + [("b", 0)] \
            + [("c", CT + k) for k in range(CT)]
        at = {key: i for i, key in enumerate(loads)}

        def slot(key):
            return ring[:, at[key] % RING, 0:(KT * AG if key[0] == "a" else D)]

        def arrived(eng, key):
            eng.wait_ge(ring_in[at[key] % RING], 16 * (at[key] // RING + 1))

        block = stack.enter_context(nc.Block())

        @block.sync
        def _(sp):
            for i, s in enumerate(scales):
                sp.dma_start(q_in[:, i:i + 1], s.rearrange("(a b) -> a b", a=1).broadcast_to([P, 1])).then_inc(q_loaded, 16)

            def load_x(t):
                sp.dma_start(x_sb[:, t, :], x_d[t]).then_inc(x_in[t], 16)

            def load_ring(key):
                i = at[key]
                if i >= RING:
                    kind, k = loads[i - RING]
                    if kind == "c":
                        sp.wait_ge(c2_ready, k + 1)
                    elif kind == "w":
                        sp.wait_ge(wlo_ready, k + 1)
                    elif kind == "a":
                        sp.wait_ge(ag_ready, 1)
                    else:
                        sp.wait_ge(blo_ready, 1)
                kind, k = key
                src = ctx_d[k] if kind == "c" else w_d[k] if kind == "w" else ag_t if kind == "a" else b_t
                sp.dma_start(slot(key), src).then_inc(ring_in[i % RING], 16)

            load_x(0)
            load_x(1)
            for k in range(CT):
                load_ring(("c", k))
                if k == 3:
                    load_x(2)
                if k == 5:
                    load_x(3)
            load_ring(("a", 0))
            for k in range(KT):
                load_ring(("w", k))
            load_ring(("b", 0))
            sp.dma_start(bias[:, :], base_b.rearrange("(a d) -> a d", a=1).broadcast_to([P, D])).then_inc(bias_in, 16)
            for t in range(TPB, TILES):
                load_x(t)
            for k in range(CT):
                load_ring(("c", CT + k))
            for t in range(TILES):
                for h in range(2):
                    cols = slice(h * HALF, (h + 1) * HALF)
                    sp.wait_ge(out_ready, 2 * t + h + 1)
                    sp.dma_start(out_d[t][:, cols], x_sb[:, t, cols]).then_inc(stored, 16)
            sp.wait_ge(stored, 32 * TILES)

        @block.gpsimd
        def _(pool):
            steps = [0]

            def chain(ins):
                steps[0] += 1
                ins.then_inc(pool_step, 1)
                pool.wait_ge(pool_step, steps[0])

            chain(pool.memset(ident_f[:, :], 0.0))
            pool.affine_select(out=ident_f[:, :], in_=ident_f[:, :], compare_op=ALU.not_equal, fill=1.0, base=0,
                               pattern=[[-1, P]], channel_multiplier=1).then_inc(consts, 1)
            pool.wait_ge(consts, 1)
            pool.tensor_copy(ident_b[:, :], ident_f[:, :]).then_inc(consts, 1)
            pool.memset(ones_b[:, :], 1.0).then_inc(consts, 1)
            pool.memset(ones_r[:, :].bitcast(F32), 1.0).then_inc(consts, 1)
            for e in range(E):
                pool.memset(iota[:, e:e + 1], float(e)).then_inc(consts, 1)

            def finish_context(k):
                pool.wait_ge(cround_ready, k + 1)
                if k >= CT:
                    pool.wait_ge(att_done, TPB)
                pool.tensor_scalar(c2[:, k % CT, :], slot(("c", k)), -(ROUND + CENTRE), 1.0,
                                   ALU.add, ALU.mult).then_inc(c2_ready, 1)

            def sum_context():
                pool.wait_ge(c2_ready, 2 * CT)
                for k in range(1, CT):
                    a = c2[:, 0, :] if k == 1 else csum[:, :].bitcast(F32)
                    ins = pool.tensor_tensor(csum[:, :], a, c2[:, k, :], ALU.add)
                    if k < CT - 1:
                        chain(ins)
                ins.then_inc(csum_ready, 1)

            def add_zfix(t):
                pool.wait_ge(att_taken, 2 * t + 2)
                pool.wait_ge(zfix_ready, 2 * (t // TPB) + 2)
                pool.tensor_tensor(x_sb[:, t, :], x_sb[:, t, :], zfix[:, :], ALU.add).then_inc(x1_ready, 1)

            def add_bias(t):
                if t == 0:
                    pool.wait_ge(bias_in, 16)
                pool.wait_ge(y_ready, t + 1)
                pool.tensor_tensor(x_sb[:, t, :], x_sb[:, t, :], bias[:, :], ALU.add).then_inc(xb_ready, 1)

            for k in range(CT):
                finish_context(k)
            for t in range(TPB):
                add_zfix(t)
            add_bias(0)
            add_bias(1)
            for k in range(CT):
                finish_context(CT + k)
            sum_context()
            add_bias(2)
            add_bias(3)
            for t in range(TPB, TILES):
                add_zfix(t)
                add_bias(t)

        @block.scalar
        def _(act):
            def first_guess(ln, t):
                act.wait_ge(var_ready[ln], t + 1)
                act.activation(ln_v[:, ln, t:t + 1], ve[:, ln, t:t + 1], ACT.Ln).then_inc(logv_ready[ln], 1)
                act.wait_ge(logv_ready[ln], t + 1)
                act.activation(r0[:, ln, t:t + 1], ln_v[:, ln, t:t + 1], ACT.Exp,
                               scale=-0.5).then_inc(r0_ready[ln], 1)

            def relu_x(t):
                act.wait_ge(q_ready, 1)
                act.wait_ge(xn_ready, t + 1)
                act.activation(xq[:, t % 2, :], xq[:, t % 2, :], ACT.Relu, bias=q_in[:, 1:2],
                               scale=q_rec[:, 0:1]).then_inc(xrelu_ready, 1)

            def integers_x(t):
                act.wait_ge(xround_ready, t + 1)
                if t >= 2:
                    act.wait_ge(c1t_psum, t - 1)
                act.activation(c1[:, t % 2, :], xq[:, t % 2, :], ACT.Copy, bias=-(ROUND + CENTRE),
                               accum_out=rowsum[:, t:t + 1]).then_inc(c1_ready, 1)
                act.wait_ge(c1_ready, t + 1)
                act.mul(rowfix[:, t:t + 1], rowsum[:, t:t + 1], ssd2).then_inc(rowfix_ready, 1)

            def take_c1t(t):
                act.wait_ge(c1t_psum, t + 1)
                if t >= 4:
                    act.wait_ge(att_done, t - 3)
                act.activation(c1t[:, t % 4].rearrange("p k m -> p (k m)"), ps_tb, ACT.Copy).then_inc(c1t_ready, 1)

            def relu_context(k):
                act.wait_ge(q_ready, 1)
                arrived(act, ("c", k))
                act.activation(slot(("c", k)), slot(("c", k)), ACT.Relu, bias=q_in[:, 3:4],
                               scale=q_rec[:, 2:3]).then_inc(crelu_ready, 1)

            def zero_point_columns(b):
                act.wait_ge(colsum_psum, b + 1)
                if b == 1:
                    act.wait_ge(x1_ready, TPB)
                for h in range(2):
                    bank = ps_even[h] if b == 0 else ps_att[h]
                    act.activation(zfix[:, h * HALF:(h + 1) * HALF], bank[:, :], ACT.Identity, bias=ssdd,
                                   scale=ssd1).then_inc(zfix_ready, 1)

            def split_w_hi(k):
                arrived(act, ("w", k))
                act.activation(w_hi[:, k, :], slot(("w", k)), ACT.Copy).then_inc(whi_ready, 1)

            def split_b_hi():
                arrived(act, ("b", 0))
                act.activation(b_hi[:, :], slot(("b", 0)), ACT.Copy).then_inc(bhi_ready, 1)

            def split_ag_hi():
                arrived(act, ("a", 0))
                act.activation(ag_hi[:, :, :].rearrange("p k n -> p (k n)"), slot(("a", 0)), ACT.Copy).then_inc(ag_hi_ready, 1)

            def split_y_hi(t, g):
                act.wait_ge(yt_psum, 2 * t + g + 1)
                if t >= 2:
                    act.wait_ge(ffn_done, t - 1)
                act.activation(yt_hi[:, t % 2, 4 * g:4 * g + 4, :].rearrange("p k m -> p (k m)"), ps_t[:, :],
                               ACT.Copy).then_inc(yhi_ready, 1)

            def exp_gate(t):
                act.wait_ge(top_ready, t + 1)
                act.activation(ex[:, :], top[:, 0:1], ACT.Exp, bias=top[:, 1:2], scale=-1.0).then_inc(ex_ready, 1)

            def split_low_hi(t):
                act.wait_ge(lowt_psum, t + 1)
                if t >= 1:
                    act.wait_ge(ffn_done, t)
                act.activation(lt_hi[:, :], low_t, ACT.Copy).then_inc(lthi_ready, 1)

            first_guess(0, 0)
            relu_x(0)
            first_guess(0, 1)
            relu_x(1)
            integers_x(0)
            take_c1t(0)
            relu_context(0)
            integers_x(1)
            take_c1t(1)
            for k in range(1, 6):
                relu_context(k)
            first_guess(0, 2)
            relu_x(2)
            relu_context(6)
            integers_x(2)
            relu_context(7)
            first_guess(0, 3)
            relu_x(3)
            take_c1t(2)
            integers_x(3)
            take_c1t(3)
            zero_point_columns(0)
            split_ag_hi()
            split_w_hi(0)
            first_guess(1, 0)
            split_w_hi(1)
            split_y_hi(0, 0)
            split_y_hi(0, 1)
            for k in range(2, KT):
                split_w_hi(k)
            split_b_hi()
            exp_gate(0)
            first_guess(1, 1)
            split_y_hi(1, 0)
            split_low_hi(0)
            split_y_hi(1, 1)
            for k in range(CT):
                relu_context(CT + k)
            exp_gate(1)
            first_guess(1, 2)
            split_y_hi(2, 0)
            split_low_hi(1)
            split_y_hi(2, 1)
            first_guess(0, 4)
            relu_x(4)
            integers_x(4)
            take_c1t(4)
            zero_point_columns(1)
            for t in range(2, TILES):
                exp_gate(t)
                if t + 1 < TILES:
                    first_guess(1, t + 1)
                    split_y_hi(t + 1, 0)
                split_low_hi(t)
                if t + 1 < TILES:
                    split_y_hi(t + 1, 1)
                if t + 3 < TILES:
                    first_guess(0, t + 3)
                    relu_x(t + 3)
                    integers_x(t + 3)
                    take_c1t(t + 3)

        @block.vector
        def _(dve):
            steps = [0]

            def chain(ins):
                steps[0] += 1
                ins.then_inc(dve_step, 1)
                dve.wait_ge(dve_step, steps[0])

            def quant_constants():
                dve.wait_ge(q_loaded, 64)
                dve.reciprocal(q_rec[:, :], q_in[:, :]).then_inc(q_ready, 1)
                chain(dve.tensor_scalar(q_d[:, :], q_in[:, :], -1.0, CENTRE, ALU.mult, ALU.add))
                chain(dve.tensor_tensor(ss, q_in[:, 0:1], q_in[:, 2:3], ALU.mult))
                chain(dve.tensor_tensor(ssd1, ss, q_d[:, 1:2], ALU.mult))
                chain(dve.tensor_tensor(ssd2, ss, q_d[:, 3:4], ALU.mult))
                dve.tensor_scalar(ssdd, ssd1, q_d[:, 3:4], float(S2), ALU.mult, ALU.mult).then_inc(q_ready, 1)

            def variance(ln, t):
                if ln == 0:
                    dve.wait_ge(x_in[t], 16)
                else:
                    dve.wait_ge(x1_ready, t + 1)
                for h in range(2):
                    ins = dve.bn_stats(stats[:, h, :], x_sb[:, t, h * HALF:(h + 1) * HALF])
                    chain(ins)
                chain(dve.bn_aggr(mv[:, ln, t, :], stats[:, :, :].rearrange("p a b -> p (a b)")))
                dve.tensor_scalar(ve[:, ln, t:t + 1], mv[:, ln, t, 1:2], EPS, None, ALU.add).then_inc(var_ready[ln], 1)

            def sharpen(ln, t):
                v, r = ve[:, ln, t:t + 1], r0[:, ln, t:t + 1]
                dve.wait_ge(r0_ready[ln], t + 1)
                chain(dve.scalar_tensor_tensor(out=r_n[:, ln, t:t + 1], in0=r, scalar=r, in1=v,
                                               op0=ALU.mult, op1=ALU.mult))
                chain(dve.tensor_scalar(r_h[:, ln, t:t + 1], r_n[:, ln, t:t + 1], -0.5, 1.5, ALU.mult, ALU.add))
                chain(dve.tensor_tensor(rstd[:, ln, t:t + 1], r_h[:, ln, t:t + 1], r, ALU.mult))

            def normalise_x(t):
                sharpen(0, t)
                if t >= 2:
                    dve.wait_ge(c1_ready, t - 1)
                dve.tensor_scalar(xq[:, t % 2, :], x_sb[:, t, :], mv[:, 0, t, 0:1], rstd[:, 0, t:t + 1],
                                  ALU.subtract, ALU.mult).then_inc(xn_ready, 1)

            def round_x(t):
                dve.wait_ge(xrelu_ready, t + 1)
                dve.tensor_scalar(xq[:, t % 2, :], xq[:, t % 2, :], QMAX, ROUND, ALU.min,
                                  ALU.add).then_inc(xround_ready, 1)

            def round_context(k):
                dve.wait_ge(crelu_ready, k + 1)
                dve.tensor_scalar(slot(("c", k)), slot(("c", k)), QMAX, ROUND, ALU.min,
                                  ALU.add).then_inc(cround_ready, 1)

            def add_attention(t):
                dve.wait_ge(att_done, t + 1)
                if t == 0:
                    dve.wait_ge(q_ready, 2)
                for h in range(2):
                    cols = slice(h * HALF, (h + 1) * HALF)
                    ins = dve.scalar_tensor_tensor(out=x_sb[:, t, cols], in0=att_bank(t)[h][:, :], scalar=ss,
                                                   in1=x_sb[:, t, cols], op0=ALU.mult, op1=ALU.add)
                    ins.then_inc(att_taken, 1)

            def normalise_x1(t):
                sharpen(1, t)
                if t >= 1:
                    dve.wait_ge(yt_psum, 2 * t)
                dve.tensor_scalar(y[:, :], x_sb[:, t, :], mv[:, 1, t, 0:1], rstd[:, 1, t:t + 1],
                                  ALU.subtract, ALU.mult).then_inc(y_ready, 1)

            def split_y_lo(t, g):
                dve.wait_ge(yhi_ready, 2 * t + g + 1)
                ks = slice(4 * g, 4 * g + 4)
                dve.tensor_tensor(yt_lo[:, t % 2, ks, :].rearrange("p k m -> p (k m)"), ps_t[:, :],
                                  yt_hi[:, t % 2, ks, :].rearrange("p k m -> p (k m)").bitcast(F32),
                                  ALU.subtract).then_inc(ylo_ready, 1)

            def split_w_lo(k):
                dve.wait_ge(whi_ready, k + 1)
                dve.tensor_tensor(w_lo[:, k, :], slot(("w", k)), w_hi[:, k, :].bitcast(F32),
                                  ALU.subtract).then_inc(wlo_ready, 1)

            def split_ag_lo():
                dve.wait_ge(ag_hi_ready, 1)
                dve.tensor_tensor(ag_lo[:, :, :].rearrange("p k n -> p (k n)"), slot(("a", 0)),
                                  ag_hi[:, :, :].rearrange("p k n -> p (k n)").bitcast(F32),
                                  ALU.subtract).then_inc(ag_ready, 1)

            def split_b_lo():
                dve.wait_ge(bhi_ready, 1)
                dve.tensor_tensor(b_lo[:, :], slot(("b", 0)), b_hi[:, :].bitcast(F32),
                                  ALU.subtract).then_inc(blo_ready, 1)

            def top_logits(t):
                dve.wait_ge(ag_done, t + 1)
                chain(dve.tensor_copy(lg[:, :], ps_g[:, ER:AG]))
                dve.max(top[:, :], lg[:, :]).then_inc(top_ready, 1)
                dve.wait_ge(top_ready, t + 1)
                chain(dve.max_index(top_i[:, :], top[:, :], lg[:, :]))
                chain(dve.tensor_copy(top_f[:, :], top_i[:, 0:2]))

            def weigh_low(t):
                dve.wait_ge(ex_ready, t + 1)
                chain(dve.tensor_scalar(den[:, :], ex[:, :], 1.0, 1.0 / SCALING, ALU.add, ALU.mult))
                chain(dve.reciprocal(wts[:, 0:1], den[:, :]))
                chain(dve.tensor_tensor(wts[:, 1:2], wts[:, 0:1], ex[:, :], ALU.mult))
                for i in range(2):
                    chain(dve.tensor_scalar(hot[:, i, :], iota[:, :], top_f[:, i:i + 1], wts[:, i:i + 1],
                                            ALU.is_equal, ALU.mult))
                chain(dve.tensor_tensor(hot[:, 2, :], hot[:, 0, :], hot[:, 1, :], ALU.add))
                if t >= 1:
                    dve.wait_ge(lowt_psum, t)
                dve.tensor_tensor(low_w[:, :].rearrange("p (e r) -> p e r", e=E),
                                  ps_g[:, 0:ER].rearrange("p (e r) -> p e r", e=E),
                                  hot[:, 2, :].unsqueeze(2).broadcast_to([P, E, R]), ALU.mult).then_inc(loww_ready, 1)

            def split_low_lo(t):
                dve.wait_ge(lthi_ready, t + 1)
                dve.tensor_tensor(lt_lo[:, :], low_t, lt_hi[:, :].bitcast(F32), ALU.subtract).then_inc(ltlo_ready, 1)

            def finish_tile(t):
                dve.wait_ge(ffn_done, t + 1)
                dve.wait_ge(xb_ready, t + 1)
                dve.wait_ge(rowfix_ready, t + 1)
                for h in range(2):
                    cols = slice(h * HALF, (h + 1) * HALF)
                    dve.scalar_tensor_tensor(out=x_sb[:, t, cols], in0=ffn_bank[t % 2][h][:, :],
                                             scalar=rowfix[:, t:t + 1], in1=x_sb[:, t, cols],
                                             op0=ALU.add, op1=ALU.add).then_inc(out_ready, 1)

            quant_constants()
            variance(0, 0)
            normalise_x(0)
            variance(0, 1)
            round_x(0)
            normalise_x(1)
            round_x(1)
            for k in range(4):
                round_context(k)
            variance(0, 2)
            round_context(4)
            round_context(5)
            normalise_x(2)
            variance(0, 3)
            round_x(2)
            round_context(6)
            normalise_x(3)
            round_context(7)
            round_x(3)
            add_attention(0)
            add_attention(1)
            split_ag_lo()
            variance(1, 0)
            split_w_lo(0)
            normalise_x1(0)
            add_attention(2)
            split_w_lo(1)
            split_y_lo(0, 0)
            split_y_lo(0, 1)
            split_w_lo(2)
            add_attention(3)
            for k in range(3, KT):
                split_w_lo(k)
            split_b_lo()
            top_logits(0)
            variance(1, 1)
            weigh_low(0)
            normalise_x1(1)
            split_y_lo(1, 0)
            split_low_lo(0)
            split_y_lo(1, 1)
            finish_tile(0)
            for k in range(CT):
                round_context(CT + k)
            top_logits(1)
            variance(1, 2)
            weigh_low(1)
            normalise_x1(2)
            split_y_lo(2, 0)
            split_low_lo(1)
            split_y_lo(2, 1)
            variance(0, 4)
            normalise_x(4)
            round_x(4)
            finish_tile(1)
            for t in range(2, TILES):
                if t + 2 < TILES:
                    add_attention(t + 2)
                if t + 1 < TILES:
                    variance(1, t + 1)
                top_logits(t)
                if t + 3 < TILES:
                    variance(0, t + 3)
                weigh_low(t)
                if t + 1 < TILES:
                    normalise_x1(t + 1)
                    split_y_lo(t + 1, 0)
                split_low_lo(t)
                if t + 1 < TILES:
                    split_y_lo(t + 1, 1)
                if t + 3 < TILES:
                    normalise_x(t + 3)
                    round_x(t + 3)
                finish_tile(t)

        @block.tensor
        def _(pe):
            t_bank_free = [None]

            def wait_t_bank():
                if t_bank_free[0] is not None:
                    pe.wait_ge(*t_bank_free[0])

            def transpose_c1(t):
                wait_t_bank()
                pe.wait_ge(c1_ready, t + 1)
                for k in range(KT):
                    ins = pe.transpose(ps_tb[:, k * P:(k + 1) * P], c1[:, t % 2, k * P:(k + 1) * P], ident_b[:, :])
                ins.then_inc(c1t_psum, 1)
                t_bank_free[0] = (c1t_ready, t + 1)

            def transpose_y(t, g):
                wait_t_bank()
                pe.wait_ge(y_ready, t + 1)
                for k in range(4 * g, 4 * g + 4):
                    ins = pe.transpose(ps_t[:, (k % 4) * P:(k % 4 + 1) * P], y[:, k * P:(k + 1) * P], ident_f[:, :])
                ins.then_inc(yt_psum, 1)
                t_bank_free[0] = (ylo_ready, 2 * t + g + 1)

            def attention(t, k):
                pe.wait_ge(c2_ready, CT * (t // TPB) + k + 1)
                if k == 0:
                    pe.wait_ge(c1t_ready, t + 1)
                    if 2 <= t < TPB:
                        pe.wait_ge(att_taken, 2 * t - 2)
                    if t == TPB:
                        pe.wait_ge(zfix_ready, 4)
                    if t > TPB:
                        pe.wait_ge(att_taken, 2 * t)
                for h in range(2):
                    ins = pe.matmul(att_bank(t)[h][:, :], c1t[:, t % 4, k, :], c2[:, k, h * HALF:(h + 1) * HALF],
                                    start=(k == 0), stop=(k == CT - 1))
                if k == CT - 1:
                    ins.then_inc(att_done, 1)

            def column_sums(b):
                if b == 1:
                    pe.wait_ge(csum_ready, 1)
                    pe.wait_ge(att_taken, 2 * TPB)
                    for h in range(2):
                        ins = pe.matmul(ps_att[h][:, :], ones_r[:, :], csum[:, h * HALF:(h + 1) * HALF],
                                        start=True, stop=True)
                    ins.then_inc(colsum_psum, 1)

            def column_sums_of(k):
                for h in range(2):
                    ins = pe.matmul(ps_even[h][:, :], ones_b[:, :], c2[:, k, h * HALF:(h + 1) * HALF],
                                    start=(k == 0), stop=(k == CT - 1))
                if k == CT - 1:
                    ins.then_inc(colsum_psum, 1)

            def low_and_gate(t):
                pe.wait_ge(ylo_ready, 2 * t + 2)
                if t == 0:
                    pe.wait_ge(ag_ready, 1)
                else:
                    pe.wait_ge(ltlo_ready, t)
                for k in range(KT):
                    h, l = yt_hi[:, t % 2, k, :], yt_lo[:, t % 2, k, :]
                    pe.matmul(ps_g[:, 0:AG], h, ag_hi[:, k, :], start=(k == 0), stop=False)
                    pe.matmul(ps_g[:, 0:AG], h, ag_lo[:, k, :], start=False, stop=False)
                    ins = pe.matmul(ps_g[:, 0:AG], l, ag_hi[:, k, :], start=False, stop=(k == KT - 1))
                ins.then_inc(ag_done, 1)

            def base(t, k):
                if t == 0:
                    pe.wait_ge(wlo_ready, k + 1)
                if k == 0:
                    if t == 0:
                        pe.wait_ge(zfix_ready, 2)
                    elif t == 1:
                        pe.wait_ge(att_taken, 2 * TPB)
                    else:
                        pe.wait_ge(out_ready, 2 * (t - 1))
                for a, b in ((yt_hi, w_hi), (yt_hi, w_lo), (yt_lo, w_hi)):
                    for h in range(2):
                        pe.matmul(ffn_bank[t % 2][h][:, :], a[:, t % 2, k, :], b[:, k, h * HALF:(h + 1) * HALF],
                                  start=(k == 0 and a is yt_hi and b is w_hi), stop=False)

            def transpose_low(t):
                pe.wait_ge(loww_ready, t + 1)
                pe.transpose(low_t, low_w[:, :], ident_f[:, :]).then_inc(lowt_psum, 1)

            def lora(t):
                pe.wait_ge(ltlo_ready, t + 1)
                if t == 0:
                    pe.wait_ge(blo_ready, 1)
                for h in range(2):
                    cols = slice(h * HALF, (h + 1) * HALF)
                    bank = ffn_bank[t % 2][h][:, :]
                    pe.matmul(bank, lt_hi[:, :], b_hi[:, cols], start=False, stop=False)
                    pe.matmul(bank, lt_hi[:, :], b_lo[:, cols], start=False, stop=False)
                    ins = pe.matmul(bank, lt_lo[:, :], b_hi[:, cols], start=False, stop=True)
                ins.then_inc(ffn_done, 1)

            pe.wait_ge(consts, 4)
            transpose_c1(0)
            transpose_c1(1)
            for k in range(CT):
                attention(0, k)
                attention(1, k)
                column_sums_of(k)
            transpose_c1(2)
            transpose_c1(3)
            for k in range(CT):
                attention(2, k)
            for k in range(CT):
                attention(3, k)
            transpose_y(0, 0)
            transpose_y(0, 1)
            for t in range(TILES):
                low_and_gate(t)
                for k in range(KT):
                    base(t, k)
                    if t + 1 < TILES and k == 3:
                        transpose_y(t + 1, 0)
                    if t + 1 < TILES and k == 5:
                        transpose_y(t + 1, 1)
                    if k == 4:
                        transpose_low(t)
                    if k == 6 and 1 <= t <= TPB:
                        transpose_c1(t + TPB - 1)
                    if k == 6 and t == 1:
                        column_sums(1)
                lora(t)
                if 1 <= t <= TPB:
                    for k in range(CT):
                        attention(t + TPB - 1, k)


_SCALES = ("L0_xattn_x1_scale", "L0_xattn_x1_zp", "L0_xattn_x2_scale", "L0_xattn_x2_zp")


def kernel(**inputs):
    import numpy as _np
    import concourse.bacc as _bacc
    from concourse import mybir as _mybir
    from concourse.bass_utils import run_bass_kernel_spmd as _run

    x = _np.ascontiguousarray(inputs["x"])
    d = x.shape[-1]
    gate_w = _np.asarray(inputs["L0_ffn_gate_w"])
    lora_a = _np.asarray(inputs["L0_ffn_lora_A"]).reshape(-1, d)
    lora_b = _np.asarray(inputs["L0_ffn_lora_B"])
    ag = _np.concatenate([lora_a, gate_w]).T.reshape(d // P, P, -1).transpose(1, 0, 2).reshape(P, -1)
    laid = {"in_x": x, "in_ctx": inputs["ctx_4096"]}
    for name in _SCALES:
        laid["in_" + name] = inputs[name]
    laid["in_w_t"] = _np.asarray(inputs["L0_ffn_base_w"]).T
    laid["in_ag_t"] = ag
    laid["in_b_t"] = lora_b.transpose(0, 2, 1).reshape(-1, lora_b.shape[1])
    laid["in_base_b"] = inputs["L0_ffn_base_b"]
    laid = {name: _np.ascontiguousarray(a) for name, a in laid.items()}

    nc = _bacc.Bacc("TRN2", target_bir_lowering=False, num_devices=1)
    aps = {name: nc.dram_tensor(name, a.shape, _mybir.dt.from_np(a.dtype), kind="ExternalInput").ap()
           for name, a in laid.items()}
    out = nc.dram_tensor("out_x", x.shape, _mybir.dt.float32, kind="ExternalOutput").ap()
    xattn_ffn(nc, aps["in_x"], aps["in_ctx"], [aps["in_" + n] for n in _SCALES], aps["in_w_t"], aps["in_ag_t"],
              aps["in_b_t"], aps["in_base_b"], out)
    r = _run(nc, [laid], core_ids=[0])
    return r.results[0]["out_x"]
```

```python
from contextlib import ExitStack

import concourse.bass as bass
from concourse import mybir

F32 = mybir.dt.float32
F32R = mybir.dt.float32r
F16 = mybir.dt.float16
U32 = mybir.dt.uint32
ALU = mybir.AluOpType
ACT = mybir.ActivationFunctionType

P = 128
HALF = 512
QMAX = 255.0
CENTRE = 128.0
ROUND = 1.5 * 2.0 ** 23
EPS = 1e-5
SCALING = 2.0
RING = 5
DVE_CONTEXT = (3,)
POOL_WEIGHTS = (0, 1, 3, 5, 7)


def xattn_ffn(nc, x, ctx, scales, w_t, ag_t, b_t, base_b, out):
    NB, S, D = x.shape
    S2 = ctx.shape[1]
    TILES = NB * S // P
    TPB = S // P
    KT = D // P
    CT = S2 // P
    AG = ag_t.shape[1] // KT
    ER = b_t.shape[0]
    E = AG - ER
    R = ER // E
    assert ER == P and D == 2 * HALF and CT == KT

    x_d = x.rearrange("b (t p) d -> (b t) p d", p=P)
    out_d = out.rearrange("b (t p) d -> (b t) p d", p=P)
    ctx_d = ctx.rearrange("b (k p) d -> (b k) p d", p=P)
    w_d = w_t.rearrange("(k p) o -> k p o", p=P)

    with ExitStack() as stack:
        def sb(name, shape, dt):
            return stack.enter_context(nc.sbuf_tensor(name, shape, dt))

        def psum(name, shape, dt=F32):
            return stack.enter_context(nc.psum_tensor(name, shape, dt))

        def sem(name):
            return stack.enter_context(nc.semaphore(name))

        x_sb = sb("x_sb", [P, TILES, D], F32)
        ring = sb("ring", [P, RING, KT * AG], F32)
        c2 = sb("c2", [P, CT, D], F16)
        w_hi = sb("w_hi", [P, KT, D], F32R)
        w_lo = sb("w_lo", [P, KT, D], F32R)
        ag = sb("ag", [P, KT, 2, AG], F32R)
        b_hi = sb("b_hi", [P, D], F32R)
        b_lo = sb("b_lo", [P, D], F32R)
        y = sb("y", [P, D], F32)
        yt_hi = sb("yt_hi", [P, 2, KT, P], F32R)
        yt_lo = sb("yt_lo", [P, 2, KT, P], F32R)
        xq = sb("xq", [P, 2, D], F32)
        c1 = sb("c1", [P, 2, D], F16)
        c1t = sb("c1t", [P, 4, KT, P], F16)
        zfix = sb("zfix", [P, D], F32)
        bias = sb("bias", [P, D], F32)
        csum = sb("csum", [P, D], F16)
        ident_f = sb("ident_f", [P, P], F32)
        ident_h = sb("ident_h", [P, P], F16)
        ones = sb("ones", [P, P], F16)
        iota = sb("iota", [P, E], F32)
        low_w = sb("low_w", [P, ER], F32)
        lt_hi = sb("lt_hi", [P, P], F32R)
        lt_lo = sb("lt_lo", [P, P], F32R)
        q_in = sb("q_in", [P, 4], F32)
        q_rec = sb("q_rec", [P, 4], F32)
        q_d = sb("q_d", [P, 4], F32)
        q_ss = sb("q_ss", [P, 4], F32)
        stats = sb("stats", [P, 2, 6], F32)
        mv = sb("mv", [P, 2, TILES, 2], F32)
        ve = sb("ve", [P, 2, TILES], F32)
        ln_v = sb("ln_v", [P, 2, TILES], F32)
        r0 = sb("r0", [P, 2, TILES], F32)
        r_n = sb("r_n", [P, 2, TILES], F32)
        r_h = sb("r_h", [P, 2, TILES], F32)
        rstd = sb("rstd", [P, 2, TILES], F32)
        rowsum = sb("rowsum", [P, TILES], F32)
        rowfix = sb("rowfix", [P, TILES], F32)
        low_g = sb("low_g", [P, AG], F32)
        top = sb("top", [P, 8], F32)
        top_i = sb("top_i", [P, 8], U32)
        top_f = sb("top_f", [P, 2], F32)
        ex = sb("ex", [P, 1], F32)
        den = sb("den", [P, 1], F32)
        wts = sb("wts", [P, 2], F32)
        hot = sb("hot", [P, 3, E], F32)

        ps_even = [psum(f"ps_even{h}", [P, HALF]) for h in range(2)]
        ps_odd = [psum(f"ps_odd{h}", [P, HALF]) for h in range(2)]
        ps_att = [psum(f"ps_att{h}", [P, HALF]) for h in range(2)]
        ps_t = psum("ps_t", [P, HALF])
        ps_g = psum("ps_g", [P, HALF])
        ffn_bank = [ps_even, ps_odd]

        def att_bank(t):
            return ps_odd if t < TPB and t % 2 else ps_att


        def y_bank(t, g):
            return ps_g if (t, g) == (0, 1) else ps_t

        ps_th = ps_t[:, :].bitcast(F16)
        low_t = ps_g[:, HALF - P:HALF]

        x_in = [sem(f"x_in{t}") for t in range(TILES)]
        ring_in = [sem(f"ring_in{r}") for r in range(RING)]
        spare_in = [sem(f"spare_in{k}") for k in range(TILES - TPB)]
        q_loaded = sem("q_loaded")
        bias_in = sem("bias_in")
        stored = sem("stored")
        consts = sem("consts")
        q_ready = sem("q_ready")
        dve_step = sem("dve_step")
        pool_step = sem("pool_step")
        var_ready = [sem(f"var_ready{i}") for i in range(2)]
        logv_ready = [sem(f"logv_ready{i}") for i in range(2)]
        r0_ready = [sem(f"r0_ready{i}") for i in range(2)]
        xn_ready = sem("xn_ready")
        xrelu_ready = sem("xrelu_ready")
        xround_ready = sem("xround_ready")
        c1_ready = sem("c1_ready")
        c1t_psum = sem("c1t_psum")
        c1t_ready = sem("c1t_ready")
        crelu_ready = sem("crelu_ready")
        cround_ready = sem("cround_ready")
        c2_ready = sem("c2_ready")
        c2v_ready = sem("c2v_ready")
        csum_ready = sem("csum_ready")
        colsum_psum = sem("colsum_psum")
        zfix_ready = sem("zfix_ready")
        att_done = sem("att_done")
        att_taken = sem("att_taken")
        x1_ready = sem("x1_ready")
        y_ready = sem("y_ready")
        xb_ready = sem("xb_ready")
        yt_psum = sem("yt_psum")
        yhi_ready = sem("yhi_ready")
        ylo_ready = sem("ylo_ready")
        ag_hi_ready = sem("ag_hi_ready")
        ag_ready = sem("ag_ready")
        whi_ready = sem("whi_ready")
        wlo_ready = sem("wlo_ready")
        wlop_ready = sem("wlop_ready")
        bhi_ready = sem("bhi_ready")
        blo_ready = sem("blo_ready")
        ag_done = sem("ag_done")
        top_ready = sem("top_ready")
        ex_ready = sem("ex_ready")
        loww_ready = sem("loww_ready")
        lowt_psum = sem("lowt_psum")
        lthi_ready = sem("lthi_ready")
        ltlo_ready = sem("ltlo_ready")
        ffn_half = sem("ffn_half")
        ffn_done = sem("ffn_done")
        rowfix_ready = sem("rowfix_ready")
        out_ready = sem("out_ready")

        pooled = [k for k in range(2 * CT) if k not in DVE_CONTEXT]

        def context_ready(eng, k):
            if k < CT:
                alone = sum(j <= k for j in DVE_CONTEXT)
                if alone:
                    eng.wait_ge(c2v_ready, alone)
            eng.wait_ge(c2_ready, sum(j <= k for j in pooled))

        def weight_ready(eng, k):
            if k in POOL_WEIGHTS:
                eng.wait_ge(wlop_ready, POOL_WEIGHTS.index(k) + 1)
            else:
                eng.wait_ge(wlo_ready, sum(j not in POOL_WEIGHTS for j in range(k + 1)))

        SPARE = TILES - TPB

        ss, ssd1, ssd2, ssdd = (q_ss[:, i:i + 1] for i in range(4))

        loads = [("c", k) for k in range(SPARE, CT)] + [("a", 0)] + [("w", k) for k in range(KT)] + [("b", 0)] \
            + [("c", CT + k) for k in range(CT)]
        at = {key: i for i, key in enumerate(loads)}

        def slot(key):
            if key not in at:
                return x_sb[:, TPB + key[1], :]
            return ring[:, at[key] % RING, 0:(KT * AG if key[0] == "a" else D)]

        def arrived(eng, key):
            if key not in at:
                eng.wait_ge(spare_in[key[1]], 16)
                return
            eng.wait_ge(ring_in[at[key] % RING], 16 * (at[key] // RING + 1))

        block = stack.enter_context(nc.Block())

        @block.sync
        def _(sp):
            def load_x(t):
                if t >= TPB:
                    context_ready(sp, t - TPB)
                sp.dma_start(x_sb[:, t, :], x_d[t]).then_inc(x_in[t], 16)

            def load_ring(key):
                i = at[key]
                if i >= RING:
                    kind, k = loads[i - RING]
                    if kind == "c":
                        context_ready(sp, k)
                    elif kind == "w":
                        weight_ready(sp, k)
                    elif kind == "a":
                        sp.wait_ge(ag_ready, 1)
                    else:
                        sp.wait_ge(blo_ready, 1)
                kind, k = key
                src = ctx_d[k] if kind == "c" else w_d[k] if kind == "w" else ag_t if kind == "a" else b_t
                sp.dma_start(slot(key), src).then_inc(ring_in[i % RING], 16)

            load_x(0)
            for i, s in enumerate(scales):
                sp.dma_start(q_in[:, i:i + 1],
                             s.rearrange("(a b) -> a b", a=1).broadcast_to([P, 1])).then_inc(q_loaded, 16)
            for k in range(CT):
                if k == 2:
                    load_x(1)
                if k < SPARE:
                    sp.dma_start(slot(("c", k)), ctx_d[k]).then_inc(spare_in[k], 16)
                else:
                    load_ring(("c", k))
            load_x(2)
            load_x(3)
            load_ring(("a", 0))
            for k in range(KT):
                load_ring(("w", k))
            load_ring(("b", 0))
            sp.dma_start(bias[:, :], base_b.rearrange("(a d) -> a d", a=1).broadcast_to([P, D])).then_inc(bias_in, 16)
            load_x(4)
            load_x(5)
            for k in range(CT):
                load_ring(("c", CT + k))
            load_x(6)
            load_x(7)
            for t in range(TILES):
                for h in range(2):
                    cols = slice(h * HALF, (h + 1) * HALF)
                    sp.wait_ge(out_ready, 2 * t + h + 1)
                    sp.dma_start(out_d[t][:, cols], x_sb[:, t, cols]).then_inc(stored, 16)
            sp.wait_ge(stored, 32 * TILES)

        @block.gpsimd
        def _(pool):
            steps = [0]

            def chain(ins):
                steps[0] += 1
                ins.then_inc(pool_step, 1)
                pool.wait_ge(pool_step, steps[0])

            chain(pool.memset(ident_f[:, :], 0.0))
            pool.affine_select(out=ident_f[:, :], in_=ident_f[:, :], compare_op=ALU.not_equal, fill=1.0, base=0,
                               pattern=[[-1, P]], channel_multiplier=1).then_inc(consts, 1)
            pool.wait_ge(consts, 1)
            pool.tensor_copy(ident_h[:, :], ident_f[:, :]).then_inc(consts, 1)
            pool.memset(ones[:, :], 1.0).then_inc(consts, 1)
            for e in range(E):
                pool.memset(iota[:, e:e + 1], float(e)).then_inc(consts, 1)

            def finish_context(k):
                pool.wait_ge(cround_ready, pooled.index(k) + 1)
                if k >= CT:
                    pool.wait_ge(att_done, TPB)
                pool.tensor_scalar(c2[:, k % CT, :], slot(("c", k)), -(ROUND + CENTRE), 1.0,
                                   ALU.add, ALU.mult).then_inc(c2_ready, 1)

            def add_zfix(t):
                pool.wait_ge(att_taken, 2 * t + 2)
                pool.wait_ge(zfix_ready, 2 * (t // TPB) + 2)
                pool.tensor_tensor(x_sb[:, t, :], x_sb[:, t, :], zfix[:, :], ALU.add).then_inc(x1_ready, 1)

            def add_bias(t):
                if t == 0:
                    pool.wait_ge(bias_in, 16)
                    pool.wait_ge(x1_ready, 1)
                pool.wait_ge(y_ready, t + 1)
                pool.tensor_tensor(x_sb[:, t, :], x_sb[:, t, :], bias[:, :], ALU.add).then_inc(xb_ready, 1)

            def sum_context(k):
                a = c2[:, 0, :] if k == 1 else csum[:, :]
                if k > 1:
                    pool.wait_ge(csum_ready, k - 1)
                pool.wait_ge(c2_ready, len(pooled) - CT + k + 1)
                pool.tensor_tensor(csum[:, :], a, c2[:, k, :], ALU.add).then_inc(csum_ready, 1)

            def split_w_lo(k):
                pool.wait_ge(whi_ready, k + 1)
                pool.tensor_tensor(w_lo[:, k, :], slot(("w", k)), w_hi[:, k, :].bitcast(F32),
                                   ALU.subtract).then_inc(wlop_ready, 1)

            def split_ag_lo():
                pool.wait_ge(ag_hi_ready, 1)
                pool.tensor_tensor(ag[:, :, 1, :], slot(("a", 0)).rearrange("p (k n) -> p k n", k=KT),
                                   ag[:, :, 0, :].bitcast(F32), ALU.subtract).then_inc(ag_ready, 1)

            for k in range(CT):
                if k in pooled:
                    finish_context(k)
            split_ag_lo()
            split_w_lo(0)
            split_w_lo(1)
            add_zfix(1)
            split_w_lo(3)
            add_zfix(2)
            split_w_lo(5)
            split_w_lo(7)
            add_zfix(3)
            finish_context(CT)
            finish_context(CT + 1)
            add_bias(0)
            finish_context(CT + 2)
            finish_context(CT + 3)
            sum_context(1)
            finish_context(CT + 4)
            finish_context(CT + 5)
            add_bias(1)
            finish_context(CT + 6)
            finish_context(CT + 7)
            for k in range(2, CT):
                sum_context(k)
            add_bias(2)
            for t in range(TPB, TILES):
                add_zfix(t)
                add_bias(t - 1)
            add_bias(TILES - 1)

        @block.scalar
        def _(act):
            def first_guess(ln, t):
                act.wait_ge(var_ready[ln], t + 1)
                act.activation(ln_v[:, ln, t:t + 1], ve[:, ln, t:t + 1], ACT.Ln).then_inc(logv_ready[ln], 1)
                act.wait_ge(logv_ready[ln], t + 1)
                act.activation(r0[:, ln, t:t + 1], ln_v[:, ln, t:t + 1], ACT.Exp,
                               scale=-0.5).then_inc(r0_ready[ln], 1)

            def relu_x(t):
                act.wait_ge(q_ready, 1)
                act.wait_ge(xn_ready, t + 1)
                act.activation(xq[:, t % 2, :], xq[:, t % 2, :], ACT.Relu, bias=q_in[:, 1:2],
                               scale=q_rec[:, 0:1]).then_inc(xrelu_ready, 1)

            def integers_x(t):
                act.wait_ge(xround_ready, t + 1)
                if t >= 2:
                    act.wait_ge(c1t_psum, t - 1)
                act.activation(c1[:, t % 2, :], xq[:, t % 2, :], ACT.Copy, bias=-(ROUND + CENTRE),
                               accum_out=rowsum[:, t:t + 1]).then_inc(c1_ready, 1)

            def zero_point_row(t):
                act.wait_ge(c1_ready, t + 1)
                act.mul(rowfix[:, t:t + 1], rowsum[:, t:t + 1], ssd2).then_inc(rowfix_ready, 1)

            def take_c1t(t):
                act.wait_ge(c1t_psum, t + 1)
                if t >= 4:
                    act.wait_ge(att_done, t - 3)
                act.activation(c1t[:, t % 4].rearrange("p k m -> p (k m)"), ps_th, ACT.Copy).then_inc(c1t_ready, 1)

            def relu_context(k):
                act.wait_ge(q_ready, 1)
                arrived(act, ("c", k))
                act.activation(slot(("c", k)), slot(("c", k)), ACT.Relu, bias=q_in[:, 3:4],
                               scale=q_rec[:, 2:3]).then_inc(crelu_ready, 1)

            def zero_point_columns(b):
                act.wait_ge(colsum_psum, b + 1)
                if b == 1:
                    act.wait_ge(x1_ready, TPB)
                for h in range(2):
                    bank = ps_even[h] if b == 0 else ps_att[h]
                    if b == 0 and h == 0:
                        act.wait_ge(q_ready, 2)
                    act.activation(zfix[:, h * HALF:(h + 1) * HALF], bank[:, :], ACT.Identity, bias=ssdd,
                                   scale=ssd1).then_inc(zfix_ready, 1)

            def split_w_hi(k):
                arrived(act, ("w", k))
                act.activation(w_hi[:, k, :], slot(("w", k)), ACT.Copy).then_inc(whi_ready, 1)

            def split_b_hi():
                arrived(act, ("b", 0))
                act.activation(b_hi[:, :], slot(("b", 0)), ACT.Copy).then_inc(bhi_ready, 1)

            def split_ag_hi():
                arrived(act, ("a", 0))
                act.activation(ag[:, :, 0, :], slot(("a", 0)).rearrange("p (k n) -> p k n", k=KT),
                               ACT.Copy).then_inc(ag_hi_ready, 1)

            def split_y_hi(t, g):
                act.wait_ge(yt_psum, 2 * t + g + 1)
                if t >= 2:
                    act.wait_ge(ffn_done, t - 1)
                act.activation(yt_hi[:, t % 2, 4 * g:4 * g + 4, :].rearrange("p k m -> p (k m)"), y_bank(t, g)[:, :],
                               ACT.Copy).then_inc(yhi_ready, 1)

            def exp_gate(t):
                act.wait_ge(top_ready, t + 1)
                act.activation(ex[:, :], top[:, 0:1], ACT.Exp, bias=top[:, 1:2], scale=-1.0).then_inc(ex_ready, 1)

            def split_low_hi(t):
                act.wait_ge(lowt_psum, t + 1)
                if t >= 1:
                    act.wait_ge(ffn_done, t)
                act.activation(lt_hi[:, :], low_t, ACT.Copy).then_inc(lthi_ready, 1)

            act.preload_act_table_set("natural_log_exp_and_others")
            first_guess(0, 0)
            relu_context(0)
            relu_x(0)
            relu_context(1)
            integers_x(0)
            relu_context(2)
            first_guess(0, 1)
            take_c1t(0)
            relu_x(1)
            relu_context(4)
            relu_context(5)
            integers_x(1)
            relu_context(6)
            relu_context(7)
            take_c1t(1)
            first_guess(0, 2)
            split_ag_hi()
            relu_x(2)
            zero_point_columns(0)
            integers_x(2)
            split_w_hi(0)
            split_w_hi(1)
            take_c1t(2)
            first_guess(1, 0)
            split_w_hi(2)
            split_w_hi(3)
            split_y_hi(0, 0)
            first_guess(0, 3)
            split_y_hi(0, 1)
            split_w_hi(4)
            relu_x(3)
            split_w_hi(5)
            integers_x(3)
            first_guess(1, 1)
            take_c1t(3)
            split_w_hi(6)
            split_w_hi(7)
            for t in range(TPB):
                zero_point_row(t)
            for t in range(TILES):
                exp_gate(t)
                if t + 1 < TILES:
                    split_y_hi(t + 1, 0)
                if t == 1:
                    relu_context(CT + 2)
                    relu_context(CT + 3)
                if 1 <= t <= TPB:
                    integers_x(t + TPB - 1)
                    zero_point_row(t + TPB - 1)
                if t + 1 < TILES:
                    split_y_hi(t + 1, 1)
                if t == 1:
                    relu_context(CT + 4)
                    relu_context(CT + 5)
                if t == 0:
                    split_b_hi()
                split_low_hi(t)
                if 1 <= t <= TPB:
                    take_c1t(t + TPB - 1)
                if t == 1:
                    relu_context(CT + 6)
                if t + 2 < TILES and t + 2 != TPB:
                    first_guess(1, t + 2)
                if t == 0:
                    relu_context(CT)
                    relu_context(CT + 1)
                if t == 1:
                    relu_context(CT + 7)
                if t == 2:
                    zero_point_columns(1)
                if t < TPB:
                    first_guess(0, t + TPB)
                    relu_x(t + TPB)
                if t == 2:
                    first_guess(1, t + 2)

        @block.vector
        def _(dve):
            steps = [0]

            def chain(ins):
                steps[0] += 1
                ins.then_inc(dve_step, 1)
                dve.wait_ge(dve_step, steps[0])

            def quant_constants():
                dve.wait_ge(q_loaded, 64)
                dve.reciprocal(q_rec[:, :], q_in[:, :]).then_inc(q_ready, 1)
                chain(dve.tensor_scalar(q_d[:, :], q_in[:, :], -1.0, CENTRE, ALU.mult, ALU.add))
                chain(dve.tensor_tensor(ss, q_in[:, 0:1], q_in[:, 2:3], ALU.mult))
                chain(dve.tensor_tensor(ssd1, ss, q_d[:, 1:2], ALU.mult))
                chain(dve.tensor_tensor(ssd2, ss, q_d[:, 3:4], ALU.mult))
                dve.tensor_scalar(ssdd, ssd1, q_d[:, 3:4], float(S2), ALU.mult, ALU.mult).then_inc(q_ready, 1)

            def variance(ln, t):
                if ln == 0:
                    dve.wait_ge(x_in[t], 16)
                else:
                    dve.wait_ge(x1_ready, t + 1)
                dve.bn_stats(stats[:, 0, :], x_sb[:, t, 0:HALF]).then_inc(dve_step, 1)
                steps[0] += 1
                chain(dve.bn_stats(stats[:, 1, :], x_sb[:, t, HALF:D]))
                chain(dve.bn_aggr(mv[:, ln, t, :], stats[:, :, :].rearrange("p a b -> p (a b)")))
                dve.tensor_scalar(ve[:, ln, t:t + 1], mv[:, ln, t, 1:2], EPS, None, ALU.add).then_inc(var_ready[ln], 1)

            def sharpen(ln, t):
                v, r = ve[:, ln, t:t + 1], r0[:, ln, t:t + 1]
                dve.wait_ge(r0_ready[ln], t + 1)
                chain(dve.scalar_tensor_tensor(out=r_n[:, ln, t:t + 1], in0=r, scalar=r, in1=v,
                                               op0=ALU.mult, op1=ALU.mult))
                chain(dve.tensor_scalar(r_h[:, ln, t:t + 1], r_n[:, ln, t:t + 1], -0.5, 1.5, ALU.mult, ALU.add))
                chain(dve.tensor_tensor(rstd[:, ln, t:t + 1], r_h[:, ln, t:t + 1], r, ALU.mult))

            def normalise_x(t):
                sharpen(0, t)
                if t >= 2:
                    dve.wait_ge(c1_ready, t - 1)
                dve.tensor_scalar(xq[:, t % 2, :], x_sb[:, t, :], mv[:, 0, t, 0:1], rstd[:, 0, t:t + 1],
                                  ALU.subtract, ALU.mult).then_inc(xn_ready, 1)

            def round_x(t):
                dve.wait_ge(xrelu_ready, t + 1)
                dve.tensor_scalar(xq[:, t % 2, :], xq[:, t % 2, :], QMAX, ROUND, ALU.min,
                                  ALU.add).then_inc(xround_ready, 1)

            def round_context(k):
                dve.wait_ge(crelu_ready, pooled.index(k) + 1)
                dve.tensor_scalar(slot(("c", k)), slot(("c", k)), QMAX, ROUND, ALU.min,
                                  ALU.add).then_inc(cround_ready, 1)

            def add_attention(t):
                dve.wait_ge(att_done, t + 1)
                if t == 0:
                    dve.wait_ge(q_ready, 2)
                for h in range(2):
                    cols = slice(h * HALF, (h + 1) * HALF)
                    ins = dve.scalar_tensor_tensor(out=x_sb[:, t, cols], in0=att_bank(t)[h][:, :], scalar=ss,
                                                   in1=x_sb[:, t, cols], op0=ALU.mult, op1=ALU.add)
                    ins.then_inc(att_taken, 1)

            def add_zfix(t):
                dve.wait_ge(zfix_ready, 2)
                dve.wait_ge(att_taken, 2 * t + 2)
                dve.tensor_tensor(x_sb[:, t, :], x_sb[:, t, :], zfix[:, :], ALU.add).then_inc(x1_ready, 1)

            def quantise_context(k):
                arrived(dve, ("c", k))
                raw = slot(("c", k))
                chain(dve.tensor_scalar(raw, raw, q_rec[:, 2:3], q_in[:, 3:4], ALU.mult, ALU.add))
                chain(dve.tensor_scalar(raw, raw, 0.0, QMAX, ALU.max, ALU.min))
                dve.tensor_scalar(c2[:, k, :], raw, ROUND, -(ROUND + CENTRE), ALU.add,
                                  ALU.add).then_inc(c2v_ready, 1)

            def normalise_x1(t):
                sharpen(1, t)
                if t >= 1:
                    dve.wait_ge(yt_psum, 2 * t)
                dve.tensor_scalar(y[:, :], x_sb[:, t, :], mv[:, 1, t, 0:1], rstd[:, 1, t:t + 1],
                                  ALU.subtract, ALU.mult).then_inc(y_ready, 1)

            def split_y_lo(t, g):
                dve.wait_ge(yhi_ready, 2 * t + g + 1)
                ks = slice(4 * g, 4 * g + 4)
                dve.tensor_tensor(yt_lo[:, t % 2, ks, :].rearrange("p k m -> p (k m)"), y_bank(t, g)[:, :],
                                  yt_hi[:, t % 2, ks, :].rearrange("p k m -> p (k m)").bitcast(F32),
                                  ALU.subtract).then_inc(ylo_ready, 1)

            def split_w_lo(k):
                dve.wait_ge(whi_ready, k + 1)
                dve.tensor_tensor(w_lo[:, k, :], slot(("w", k)), w_hi[:, k, :].bitcast(F32),
                                  ALU.subtract).then_inc(wlo_ready, 1)

            def split_b_lo():
                dve.wait_ge(bhi_ready, 1)
                dve.tensor_tensor(b_lo[:, :], slot(("b", 0)), b_hi[:, :].bitcast(F32),
                                  ALU.subtract).then_inc(blo_ready, 1)

            def top_logits(t):
                dve.wait_ge(ag_done, t + 1)
                chain(dve.tensor_copy(low_g[:, :], ps_g[:, 0:AG]))
                chain(dve.tensor_tensor(low_g[:, :], low_g[:, :], ps_g[:, AG:2 * AG], ALU.add))
                dve.max(top[:, :], low_g[:, ER:AG]).then_inc(top_ready, 1)
                dve.wait_ge(top_ready, t + 1)
                chain(dve.max_index(top_i[:, :], top[:, :], low_g[:, ER:AG]))
                chain(dve.tensor_copy(top_f[:, :], top_i[:, 0:2]))

            def weigh_low(t):
                dve.wait_ge(ex_ready, t + 1)
                chain(dve.tensor_scalar(den[:, :], ex[:, :], 1.0, 1.0 / SCALING, ALU.add, ALU.mult))
                chain(dve.reciprocal(wts[:, 0:1], den[:, :]))
                chain(dve.tensor_tensor(wts[:, 1:2], wts[:, 0:1], ex[:, :], ALU.mult))
                dve.tensor_scalar(hot[:, 0, :], iota[:, :], top_f[:, 0:1], wts[:, 0:1], ALU.is_equal,
                                  ALU.mult).then_inc(dve_step, 1)
                steps[0] += 1
                chain(dve.tensor_scalar(hot[:, 1, :], iota[:, :], top_f[:, 1:2], wts[:, 1:2], ALU.is_equal, ALU.mult))
                chain(dve.tensor_tensor(hot[:, 2, :], hot[:, 0, :], hot[:, 1, :], ALU.add))
                if t >= 1:
                    dve.wait_ge(lowt_psum, t)
                dve.tensor_tensor(low_w[:, :].rearrange("p (e r) -> p e r", e=E),
                                  low_g[:, 0:ER].rearrange("p (e r) -> p e r", e=E),
                                  hot[:, 2, :].unsqueeze(2).broadcast_to([P, E, R]), ALU.mult).then_inc(loww_ready, 1)

            def split_low_lo(t):
                dve.wait_ge(lthi_ready, t + 1)
                dve.tensor_tensor(lt_lo[:, :], low_t, lt_hi[:, :].bitcast(F32), ALU.subtract).then_inc(ltlo_ready, 1)

            def finish_tile(t):
                dve.wait_ge(xb_ready, t + 1)
                dve.wait_ge(rowfix_ready, t + 1)
                for h in range(2):
                    dve.wait_ge(ffn_done if h else ffn_half, t + 1)
                    cols = slice(h * HALF, (h + 1) * HALF)
                    dve.scalar_tensor_tensor(out=x_sb[:, t, cols], in0=ffn_bank[t % 2][h][:, :],
                                             scalar=rowfix[:, t:t + 1], in1=x_sb[:, t, cols],
                                             op0=ALU.add, op1=ALU.add).then_inc(out_ready, 1)

            variance(0, 0)
            quant_constants()
            normalise_x(0)
            round_context(0)
            round_x(0)
            round_context(1)
            variance(0, 1)
            round_context(2)
            normalise_x(1)
            quantise_context(3)
            round_x(1)
            round_context(4)
            round_context(5)
            round_context(6)
            round_context(7)
            variance(0, 2)
            normalise_x(2)
            add_attention(0)
            round_x(2)
            add_zfix(0)
            variance(1, 0)
            add_attention(1)
            normalise_x1(0)
            split_w_lo(2)
            variance(0, 3)
            split_y_lo(0, 0)
            normalise_x(3)
            split_y_lo(0, 1)
            split_w_lo(4)
            round_x(3)
            variance(1, 1)
            normalise_x1(1)
            add_attention(2)
            split_w_lo(6)
            for t in range(TILES):
                if 1 < t and t + 2 < TILES:
                    add_attention(t + 2)
                top_logits(t)
                weigh_low(t)
                if t + 1 < TILES:
                    split_y_lo(t + 1, 0)
                if t == 0:
                    add_attention(3)
                    variance(0, TPB)
                if t >= 1:
                    finish_tile(t - 1)
                if 1 <= t <= TPB:
                    round_x(t + TPB - 1)
                if t == 1:
                    round_context(CT + 2)
                    round_context(CT + 3)
                if t + 1 < TILES:
                    split_y_lo(t + 1, 1)
                if t == 0:
                    split_b_lo()
                if t == 1:
                    round_context(CT + 4)
                    round_context(CT + 5)
                if t == 1:
                    split_low_lo(t)
                if t + 2 < TILES and t + 2 != TPB:
                    variance(1, t + 2)
                if t != 1:
                    split_low_lo(t)
                if t == 1:
                    round_context(CT + 6)
                if t + 2 < TILES and t + 2 != TPB:
                    normalise_x1(t + 2)
                if t == 0:
                    round_context(CT)
                    round_context(CT + 1)
                if t == 1:
                    round_context(CT + 7)
                if 1 <= t < TPB:
                    variance(0, t + TPB)
                if t < TPB:
                    normalise_x(t + TPB)
                if t == 2:
                    variance(1, t + 2)
                    normalise_x1(t + 2)
            finish_tile(TILES - 1)

        @block.tensor
        def _(pe):
            t_bank_free = [None]

            def wait_t_bank():
                if t_bank_free[0] is not None:
                    pe.wait_ge(*t_bank_free[0])

            def transpose_c1(t):
                wait_t_bank()
                pe.wait_ge(c1_ready, t + 1)
                for k in range(KT):
                    ins = pe.transpose(ps_th[:, k * P:(k + 1) * P], c1[:, t % 2, k * P:(k + 1) * P], ident_h[:, :])
                ins.then_inc(c1t_psum, 1)
                t_bank_free[0] = (c1t_ready, t + 1)

            def transpose_y(t, g):
                if y_bank(t, g) is ps_t:
                    wait_t_bank()
                pe.wait_ge(y_ready, t + 1)
                for k in range(4 * g, 4 * g + 4):
                    ins = pe.transpose(y_bank(t, g)[:, (k % 4) * P:(k % 4 + 1) * P], y[:, k * P:(k + 1) * P], ident_f[:, :])
                ins.then_inc(yt_psum, 1)
                if y_bank(t, g) is ps_t:
                    t_bank_free[0] = (ylo_ready, 2 * t + g + 1)

            def attention(t, k):
                context_ready(pe, CT * (t // TPB) + k)
                if k == 0:
                    pe.wait_ge(c1t_ready, t + 1)
                    if 2 <= t < TPB:
                        pe.wait_ge(att_taken, 2 * t - 2)
                    if t == TPB + 1:
                        pe.wait_ge(zfix_ready, 4)
                    elif t >= TPB:
                        pe.wait_ge(att_taken, 2 * t)
                for h in range(2):
                    ins = pe.matmul(att_bank(t)[h][:, :], c1t[:, t % 4, k, :], c2[:, k, h * HALF:(h + 1) * HALF],
                                    start=(k == 0), stop=(k == CT - 1))
                if k == CT - 1:
                    ins.then_inc(att_done, 1)

            def column_sums(b):
                if b == 1:
                    pe.wait_ge(csum_ready, CT - 1)
                    pe.wait_ge(att_taken, 2 * TPB + 2)
                    for h in range(2):
                        ins = pe.matmul(ps_att[h][:, :], ones[:, :], csum[:, h * HALF:(h + 1) * HALF],
                                        start=True, stop=True)
                    ins.then_inc(colsum_psum, 1)

            def column_sums_of(k):
                for h in range(2):
                    ins = pe.matmul(ps_even[h][:, :], ones[:, :], c2[:, k, h * HALF:(h + 1) * HALF],
                                    start=(k == 0), stop=(k == CT - 1))
                if k == CT - 1:
                    ins.then_inc(colsum_psum, 1)

            def low_and_gate(t):
                pe.wait_ge(ylo_ready, 2 * t + 2)
                if t == 0:
                    pe.wait_ge(ag_ready, 1)
                else:
                    pe.wait_ge(ltlo_ready, t)
                for k in range(KT):
                    h, l = yt_hi[:, t % 2, k, :], yt_lo[:, t % 2, k, :]
                    if k == KT - 1:
                        pe.matmul(ps_g[:, 0:AG], l, ag[:, k, 0, :], start=False, stop=False)
                    ins = pe.matmul(ps_g[:, 0:2 * AG], h, ag[:, k, :, :].rearrange("p a n -> p (a n)"),
                                    start=(k == 0), stop=(k == KT - 1))
                    if k < KT - 1:
                        pe.matmul(ps_g[:, 0:AG], l, ag[:, k, 0, :], start=False, stop=False)
                ins.then_inc(ag_done, 1)

            def base(t, k):
                if t == 0:
                    weight_ready(pe, k)
                if k == 0:
                    if t == 0:
                        pe.wait_ge(zfix_ready, 2)
                    elif t == 1:
                        pe.wait_ge(att_taken, 2 * TPB)
                    else:
                        pe.wait_ge(out_ready, 2 * (t - 1))
                for a, b in ((yt_hi, w_hi), (yt_hi, w_lo), (yt_lo, w_hi)):
                    for h in range(2):
                        pe.matmul(ffn_bank[t % 2][h][:, :], a[:, t % 2, k, :], b[:, k, h * HALF:(h + 1) * HALF],
                                  start=(k == 0 and a is yt_hi and b is w_hi), stop=False)

            def transpose_low(t):
                pe.wait_ge(loww_ready, t + 1)
                pe.transpose(low_t, low_w[:, :], ident_f[:, :]).then_inc(lowt_psum, 1)

            def lora(t):
                pe.wait_ge(ltlo_ready, t + 1)
                if t == 0:
                    pe.wait_ge(blo_ready, 1)
                for h in range(2):
                    cols = slice(h * HALF, (h + 1) * HALF)
                    bank = ffn_bank[t % 2][h][:, :]
                    pe.matmul(bank, lt_hi[:, :], b_hi[:, cols], start=False, stop=False)
                    pe.matmul(bank, lt_hi[:, :], b_lo[:, cols], start=False, stop=False)
                    ins = pe.matmul(bank, lt_lo[:, :], b_hi[:, cols], start=False, stop=True)
                    if h == 0:
                        ins.then_inc(ffn_half, 1)
                ins.then_inc(ffn_done, 1)

            pe.wait_ge(consts, 3)
            transpose_c1(0)
            for k in range(CT):
                attention(0, k)
                column_sums_of(k)
                if k == 4:
                    transpose_c1(1)
            for k in range(CT):
                attention(1, k)
            transpose_c1(2)
            for k in range(CT):
                attention(2, k)
                if k == 3:
                    transpose_y(0, 0)
                if k == 5:
                    transpose_y(0, 1)
            for t in range(TILES):
                low_and_gate(t)
                for k in range(KT):
                    base(t, k)
                    if t == 0 and k == 0:
                        transpose_c1(3)
                    if t == 0 and k == 1:
                        for kc in range(CT):
                            attention(3, kc)
                    if t + 1 < TILES and k == 1:
                        transpose_y(t + 1, 0)
                    if t + 1 < TILES and k == 3:
                        transpose_y(t + 1, 1)
                    if k == 5:
                        transpose_low(t)
                    if k == 6 and 1 <= t <= TPB:
                        transpose_c1(t + TPB - 1)
                    if k == 6 and t == 2:
                        column_sums(1)
                lora(t)
                if 1 <= t <= TPB:
                    for k in range(CT):
                        attention(t + TPB - 1, k)


_SCALES = ("L0_xattn_x1_scale", "L0_xattn_x1_zp", "L0_xattn_x2_scale", "L0_xattn_x2_zp")


def kernel(**inputs):
    import numpy as _np
    import concourse.bacc as _bacc
    from concourse import mybir as _mybir
    from concourse.bass_utils import run_bass_kernel_spmd as _run

    x = _np.ascontiguousarray(inputs["x"])
    d = x.shape[-1]
    gate_w = _np.asarray(inputs["L0_ffn_gate_w"])
    lora_a = _np.asarray(inputs["L0_ffn_lora_A"]).reshape(-1, d)
    lora_b = _np.asarray(inputs["L0_ffn_lora_B"])
    ag = _np.concatenate([lora_a, gate_w]).T.reshape(d // P, P, -1).transpose(1, 0, 2).reshape(P, -1)
    laid = {"in_x": x, "in_ctx": inputs["ctx_4096"]}
    for name in _SCALES:
        laid["in_" + name] = inputs[name]
    laid["in_w_t"] = _np.asarray(inputs["L0_ffn_base_w"]).T
    laid["in_ag_t"] = ag
    laid["in_b_t"] = lora_b.transpose(0, 2, 1).reshape(-1, lora_b.shape[1])
    laid["in_base_b"] = inputs["L0_ffn_base_b"]
    laid = {name: _np.ascontiguousarray(a) for name, a in laid.items()}

    nc = _bacc.Bacc("TRN2", target_bir_lowering=False, num_devices=1)
    aps = {name: nc.dram_tensor(name, a.shape, _mybir.dt.from_np(a.dtype), kind="ExternalInput").ap()
           for name, a in laid.items()}
    out = nc.dram_tensor("out_x", x.shape, _mybir.dt.float32, kind="ExternalOutput").ap()
    xattn_ffn(nc, aps["in_x"], aps["in_ctx"], [aps["in_" + n] for n in _SCALES], aps["in_w_t"], aps["in_ag_t"],
              aps["in_b_t"], aps["in_base_b"], out)
    r = _run(nc, [laid], core_ids=[0])
    return r.results[0]["out_x"]
```
